# Optimizing a Trainium2 kernel written in Bass

```python
import numpy as np
import jax
import jax.numpy as jnp

def _softmax(x, axis=-1):
    return jax.nn.softmax(x, axis=axis)

def _gelu(x):
    return jax.nn.gelu(x, approximate=True)

def _silu(x):
    return jax.nn.silu(x)

def _sigmoid(x):
    return jax.nn.sigmoid(x)

def _layernorm(x, axis=-1, eps=1e-05):
    m = jnp.mean(x, axis=axis, keepdims=True)
    v = jnp.var(x, axis=axis, keepdims=True)
    return (x - m) / jnp.sqrt(v + eps)

def _scatter_add(tgt, idx, src, axis=0):
    return tgt.at[idx].add(src)

def _segment_sum(src, seg, n):
    return jax.ops.segment_sum(src, seg, n)
kernel_name = 'mk_gnn_resnorm_d4_gnn_r16_c6f825'

def setup_inputs(seed: int=0):
    np.random.seed(seed)
    _w = jnp.asarray

    def _rec_inputs():
        import jax
        import jax.numpy as jnp
        _gk = jax.random.key(seed)
        x = -0.000202 + 1 * jax.random.normal(jax.random.fold_in(_gk, 1), (6250, 64), jnp.float32)
        src = jax.random.randint(jax.random.fold_in(_gk, 2), (200000,), 0, 6250, jnp.int32)
        dst = jax.random.randint(jax.random.fold_in(_gk, 3), (200000,), 0, 6250, jnp.int32)
        _o = jnp.argsort(dst, stable=True)
        src = src[_o]
        dst = dst[_o]
        edge_attr_16 = 0.000196303 + 1.00016 * jax.random.normal(jax.random.fold_in(_gk, 11), (200000, 16), jnp.float32)
        edge_attr_32 = -7.08334e-05 + 0.999895 * jax.random.normal(jax.random.fold_in(_gk, 12), (200000, 32), jnp.float32)
        return (x, src, dst, edge_attr_16, edge_attr_32)
    x, src, dst, edge_attr_16, edge_attr_32 = _rec_inputs()

    def _L0_gnn_setup():
        import jax, jax.numpy as jnp
        import numpy as np
        N_NODES = 6250
        N_EDGES = 100000
        IN_CH = 64
        OUT_CH = 64
        EDGE_DIM = 16
        key = jax.random.key(seed)
        ks = jax.random.split(key, 8)
        x = jax.random.normal(ks[0], (N_NODES, IN_CH), dtype=jnp.float32)
        edge_index = jax.random.randint(ks[1], (2, N_EDGES), 0, N_NODES, dtype=jnp.int64)
        edge_attr = jax.random.normal(ks[2], (N_EDGES, EDGE_DIM), dtype=jnp.float32)
        W_l = jax.random.normal(ks[3], (IN_CH, OUT_CH), dtype=jnp.float32) / np.sqrt(IN_CH)
        b_l = jnp.zeros((OUT_CH,), dtype=jnp.float32)
        W_r = jax.random.normal(ks[4], (IN_CH, OUT_CH), dtype=jnp.float32) / np.sqrt(IN_CH)
        W_e = jax.random.normal(ks[5], (EDGE_DIM, OUT_CH), dtype=jnp.float32) / np.sqrt(EDGE_DIM)
        b_e = jax.random.normal(ks[6], (OUT_CH,), dtype=jnp.float32) * 0.01
        return {'x': x, 'edge_index': edge_index, 'edge_attr': edge_attr, 'W_l': W_l, 'b_l': b_l, 'W_r': W_r, 'W_e': W_e, 'b_e': b_e}
    _L0_gnn_all = _L0_gnn_setup()
    _L0_gnn_in = {k: v for k, v in _L0_gnn_all.items() if k in ('W_l', 'b_l', 'W_r', 'W_e', 'b_e')}
    del _L0_gnn_all

    def _L1_gnn_setup():
        import jax, jax.numpy as jnp
        import numpy as np
        N_NODES = 6250
        N_EDGES = 75000
        D_NODE = 64
        D_EDGE = 32
        N_LAYERS = 5
        key = jax.random.key(seed)
        ks = jax.random.split(key, 7)
        x = jax.random.normal(ks[0], (N_NODES, D_NODE), dtype=jnp.float32)
        edge_feats = jax.random.normal(ks[1], (N_EDGES, D_EDGE), dtype=jnp.float32)
        edge_index = jax.random.randint(ks[2], (2, N_EDGES), 0, N_NODES, dtype=jnp.int64)
        nn_w = jax.random.normal(ks[3], (N_LAYERS, D_NODE, D_NODE), dtype=jnp.float32) * 0.1
        nn_b = jax.random.normal(ks[4], (N_LAYERS, D_NODE), dtype=jnp.float32) * 0.1
        lin_w = jax.random.normal(ks[5], (N_LAYERS, D_EDGE, D_NODE), dtype=jnp.float32) * 0.1
        lin_b = jax.random.normal(ks[6], (N_LAYERS, D_NODE), dtype=jnp.float32) * 0.1
        return {'x': x, 'edge_feats': edge_feats, 'nn_w': nn_w, 'nn_b': nn_b, 'lin_w': lin_w, 'lin_b': lin_b, 'edge_index': edge_index}
    _L1_gnn_all = _L1_gnn_setup()
    _L1_gnn_in = {k: v for k, v in _L1_gnn_all.items() if k in ('nn_w', 'nn_b', 'lin_w', 'lin_b')}
    del _L1_gnn_all

    def _L2_gnn_setup():
        import jax, jax.numpy as jnp
        import numpy as np
        N_NODES = 6250
        N_EDGES = 78125
        D_IN = 64
        D_OUT = 64
        key = jax.random.key(seed)
        k1, k2, k3, k4 = jax.random.split(key, 4)
        x = jax.random.normal(k1, (N_NODES, D_IN), dtype=jnp.float32)
        edge_index = jax.random.randint(k2, (2, N_EDGES), 0, N_NODES, dtype=jnp.int64)
        weight = jax.random.normal(k3, (D_IN, D_OUT), dtype=jnp.float32) * (1.0 / np.sqrt(D_IN))
        bias = jax.random.normal(k4, (D_OUT,), dtype=jnp.float32) * 0.01
        return {'x': x, 'edge_index': edge_index, 'weight': weight, 'bias': bias}
    _L2_gnn_all = _L2_gnn_setup()
    _L2_gnn_in = {k: v for k, v in _L2_gnn_all.items() if k in ('weight', 'bias')}
    del _L2_gnn_all

    def _L3_gnn_setup():
        import jax, jax.numpy as jnp
        import numpy as np
        N_NODES = 6250
        N_EDGES = 62500
        IN_F = 64
        EDGE_F = 16
        OUT_F = 64
        EDGE_IMPORTANCE = 1.0
        BN_EPS = 1e-05
        key = jax.random.key(seed)
        k1, k2, k3, k4, k5 = jax.random.split(key, 5)
        x = jax.random.normal(k1, (N_NODES, IN_F), dtype=jnp.float32)
        edge_index = jax.random.randint(k2, (2, N_EDGES), 0, N_NODES, dtype=jnp.int64)
        edge_attr = jax.random.normal(k3, (N_EDGES, EDGE_F), dtype=jnp.float32)
        W = jax.random.normal(k4, (OUT_F, IN_F + EDGE_F), dtype=jnp.float32) * (1.0 / np.sqrt(IN_F + EDGE_F))
        b = jax.random.normal(k5, (OUT_F,), dtype=jnp.float32) * 0.01
        gamma = jnp.ones((OUT_F,), dtype=jnp.float32)
        beta = jnp.zeros((OUT_F,), dtype=jnp.float32)
        return {'x': x, 'edge_index': edge_index, 'edge_attr': edge_attr, 'W': W, 'b': b, 'gamma': gamma, 'beta': beta}
    _L3_gnn_all = _L3_gnn_setup()
    _L3_gnn_in = {k: v for k, v in _L3_gnn_all.items() if k in ('W', 'b', 'gamma', 'beta')}
    del _L3_gnn_all
    return {'x': x, 'src': src, 'dst': dst, 'edge_attr_16': edge_attr_16, 'edge_attr_32': edge_attr_32, 'L0_gnn_W_l': _L0_gnn_in['W_l'], 'L0_gnn_b_l': _L0_gnn_in['b_l'], 'L0_gnn_W_r': _L0_gnn_in['W_r'], 'L0_gnn_W_e': _L0_gnn_in['W_e'], 'L0_gnn_b_e': _L0_gnn_in['b_e'], 'L1_gnn_nn_w': _L1_gnn_in['nn_w'], 'L1_gnn_nn_b': _L1_gnn_in['nn_b'], 'L1_gnn_lin_w': _L1_gnn_in['lin_w'], 'L1_gnn_lin_b': _L1_gnn_in['lin_b'], 'L2_gnn_weight': _L2_gnn_in['weight'], 'L2_gnn_bias': _L2_gnn_in['bias'], 'L3_gnn_W': _L3_gnn_in['W'], 'L3_gnn_b': _L3_gnn_in['b'], 'L3_gnn_gamma': _L3_gnn_in['gamma'], 'L3_gnn_beta': _L3_gnn_in['beta']}

def reference(x, src, dst, edge_attr_16, edge_attr_32, L0_gnn_W_l, L0_gnn_b_l, L0_gnn_W_r, L0_gnn_W_e, L0_gnn_b_e, L1_gnn_nn_w, L1_gnn_nn_b, L1_gnn_lin_w, L1_gnn_lin_b, L2_gnn_weight, L2_gnn_bias, L3_gnn_W, L3_gnn_b, L3_gnn_gamma, L3_gnn_beta):
    import jax
    import jax.numpy as jnp

    def _L0_gnn_ref(x, edge_index, edge_attr, W_l, b_l, W_r, W_e, b_e):
        import jax, jax.numpy as jnp
        import numpy as np
        N_NODES = 6250
        N_EDGES = 100000
        IN_CH = 64
        OUT_CH = 64
        EDGE_DIM = 16
        N = x.shape[0]
        row, col = (edge_index[0], edge_index[1])
        x_j = x[row]
        agg = jax.ops.segment_sum(x_j, col, num_segments=N)
        cnt = jax.ops.segment_sum(jnp.ones((row.shape[0],), x.dtype), col, num_segments=N)
        mean = agg / jnp.maximum(cnt, 1.0)[:, None]
        out = mean @ W_l + b_l + x @ W_r
        e = edge_attr @ W_e + b_e
        out = out + jnp.zeros_like(out).at[col].set(e)
        return out

    def _L1_gnn_ref(x, edge_feats, nn_w, nn_b, lin_w, lin_b, edge_index):
        import jax, jax.numpy as jnp
        import numpy as np
        N_NODES = 6250
        N_EDGES = 75000
        D_NODE = 64
        D_EDGE = 32
        N_LAYERS = 5
        src = edge_index[0]
        dst = edge_index[1]
        n = x.shape[0]
        h = x
        for l in range(N_LAYERS):
            e = edge_feats @ lin_w[l] + lin_b[l]
            msg = jax.nn.relu(h[src] + e)
            aggr = jax.ops.segment_sum(msg, dst, num_segments=n)
            h = (h + aggr) @ nn_w[l] + nn_b[l]
            h = jax.nn.elu(h)
        return h

    def _L2_gnn_ref(x, edge_index, weight, bias):
        import jax, jax.numpy as jnp
        import numpy as np
        N_NODES = 6250
        N_EDGES = 78125
        D_IN = 64
        D_OUT = 64
        N = x.shape[0]
        h = x @ weight
        loop = jnp.arange(N, dtype=edge_index.dtype)
        row = jnp.concatenate([edge_index[0], loop])
        col = jnp.concatenate([edge_index[1], loop])
        ones = jnp.ones(row.shape[0], dtype=h.dtype)
        deg = jax.ops.segment_sum(ones, row, num_segments=N)
        deg_inv_sqrt = jax.lax.rsqrt(deg)
        norm = deg_inv_sqrt[row] * deg_inv_sqrt[col]
        out = jax.ops.segment_sum(h[col] * norm[:, None], row, num_segments=N)
        return out + bias

    def _L3_gnn_ref(x, edge_index, edge_attr, W, b, gamma, beta):
        import jax, jax.numpy as jnp
        import numpy as np
        N_NODES = 6250
        N_EDGES = 62500
        IN_F = 64
        EDGE_F = 16
        OUT_F = 64
        EDGE_IMPORTANCE = 1.0
        BN_EPS = 1e-05
        row, col = (edge_index[0], edge_index[1])
        n_nodes = x.shape[0]
        edge_features = edge_attr * EDGE_IMPORTANCE
        atom_features = x[row]
        combined = jnp.concatenate([atom_features, edge_features], -1)
        u = combined @ W.T + b
        u = jax.nn.relu(u)
        mean = jnp.mean(u, axis=0)
        var = jnp.mean((u - mean) ** 2, axis=0)
        u = (u - mean) * jax.lax.rsqrt(var + BN_EPS) * gamma + beta
        sums = jax.ops.segment_sum(u, col, num_segments=n_nodes)
        counts = jax.ops.segment_sum(jnp.ones((u.shape[0],), u.dtype), col, num_segments=n_nodes)
        aggregated = sums / jnp.maximum(counts, 1.0)[:, None]
        return aggregated + x
    edge_index = jnp.stack([src, dst])
    x = _layernorm(x + _L0_gnn_ref(x, edge_index, edge_attr_16, L0_gnn_W_l, L0_gnn_b_l, L0_gnn_W_r, L0_gnn_W_e, L0_gnn_b_e), axis=-1)
    x = _layernorm(x + _L1_gnn_ref(x, edge_attr_32, L1_gnn_nn_w, L1_gnn_nn_b, L1_gnn_lin_w, L1_gnn_lin_b, edge_index), axis=-1)
    x = _layernorm(x + _L2_gnn_ref(x, edge_index, L2_gnn_weight, L2_gnn_bias), axis=-1)
    x = _layernorm(x + _L3_gnn_ref(x, edge_index, edge_attr_16, L3_gnn_W, L3_gnn_b, L3_gnn_gamma, L3_gnn_beta), axis=-1)
    return x

_drawn_inputs = setup_inputs


def setup_inputs(seed=0):
    import zlib

    import numpy as np

    out = dict(_drawn_inputs(seed))
    spreads = {'L0_gnn_b_l': (0.0, 0.1), 'L3_gnn_gamma': (1.0, 0.2), 'L3_gnn_beta': (0.0, 0.1)}
    factors = {}
    for name, (base, spread) in spreads.items():
        noise = np.random.default_rng([zlib.crc32(name.encode()), seed]).standard_normal(out[name].shape)
        drawn = base * np.exp(spread * noise) if base else spread * noise
        out[name] = jnp.asarray(drawn.astype(out[name].dtype))
    for name, factor in factors.items():
        out[name] = (out[name] * factor).astype(out[name].dtype)
    return out
```

```python
from contextlib import ExitStack

import concourse.bass as bass
from concourse import mybir

P = 128
NODES, EDGES, F, EF16, EF32, LAYERS = 6250, 200000, 64, 16, 32, 5
BLOCKS = -(-NODES // P)
NPAD = BLOCKS * P
G = 8
TC = 16
TP = 98
TILES = TP * TC
STEPS = TILES + BLOCKS - 1
GROUPS = STEPS // G
SLOTS = 2
ITERS = GROUPS // SLOTS
SC = -(-STEPS // P)
SPAD = SC * P
TABLES = G
TRASH = P
NW = BLOCKS * F
BANK = 512
CH = 4
CHUNKS = [4] * 7 + [3] * 7
START = [sum(CHUNKS[:j]) for j in range(len(CHUNKS))]
NCH = len(CHUNKS)
assert sum(CHUNKS) == BLOCKS and NCH % 2 == 0
EPS = 1e-5
LAST_T = TILES - 1

F32, BF16, I32 = mybir.dt.float32, mybir.dt.bfloat16, mybir.dt.int32
ALU, ACT, AX = mybir.AluOpType, mybir.ActivationFunctionType, mybir.AxisListType


def free(g):
    return g + 1


def done(g):
    return g + 1 + SLOTS


def gnn(nc, x, src, dst, last, ea16, ea16t, ea32t, wl, bl, wr, we, be, nnw, nnb, linw, linb, w2, b2, w3a, w3b, b3,
        gamma, beta, out):
    with ExitStack() as ctx:
        def sb(name, shape, dt=F32):
            return ctx.enter_context(nc.sbuf_tensor(name, shape, dt))

        def sem(name):
            return ctx.enter_context(nc.semaphore(name))

        node_table = nc.dram_tensor("node_table", (NPAD, F), F32).ap()
        row_scratch = nc.dram_tensor("row_scratch", (3, SPAD), I32).ap()
        dl_rows = nc.dram_tensor("dl_rows", (SPAD, P), F32).ap()
        sr_rows = nc.dram_tensor("sr_rows", (SPAD, P), F32).ap()
        tables = [nc.dram_tensor(f"src_sums{k}", (NPAD + TRASH, F), F32).ap() for k in range(TABLES)]

        iota_row = sb("iota_row", [P, P])
        iota_p = sb("iota_p", [P, 1])
        ident = sb("ident", [P, P])
        upper = sb("upper", [P, P])
        strict = sb("strict", [P, P])
        ones = sb("ones", [P, P])
        zeros = sb("zeros", [P, BANK], BF16)
        zrow = sb("zrow", [P, F])
        w0 = sb("w0", [P, F])
        w0e = sb("w0e", [EF16 + 1, F])
        bl_b = sb("bl_b", [P, F])
        nnw_all = sb("nnw_all", [F, LAYERS * F])
        nnb_b = sb("nnb_b", [P, LAYERS * F])
        linw_all = sb("linw_all", [EF32, (LAYERS + 1) * F])
        linb_b = sb("linb_b", [P, (LAYERS + 1) * F])
        w2_sb = sb("w2_sb", [F, F])
        b2_b = sb("b2_b", [P, F])
        w3a_sb = sb("w3a_sb", [F, F])
        w3b_sb = sb("w3b_sb", [EF16, F])
        b3_b = sb("b3_b", [P, F])
        gamma_b = sb("gamma_b", [P, F])
        beta_b = sb("beta_b", [P, F])
        X = sb("X", [P, BLOCKS, F])
        H = sb("H", [P, BLOCKS, F])
        Y = sb("Y", [P, BLOCKS, F])
        CAT = sb("CAT", [P, BLOCKS, 2 * F])
        CATW = CAT[:].rearrange("p b f -> p (b f)")
        SQ = CATW[:, 0:NW].rearrange("p (b f) -> p b f", f=F)
        SQ2 = CATW[:, NW:2 * NW].rearrange("p (b f) -> p b f", f=F)
        E17 = sb("E17", [P, BLOCKS, EF16 + 1])
        EG = sb("EG", [P, BLOCKS, EF16])
        cnt = sb("cnt", [P, BLOCKS])
        deg = sb("deg", [P, BLOCKS])
        rcnt = sb("rcnt", [P, BLOCKS])
        dinv = sb("dinv", [P, BLOCKS])
        stat = sb("stat", [P, 2, BLOCKS])
        cntT = sb("cntT", [BLOCKS, P])
        cntX = sb("cntX", [P, BLOCKS])
        lastf = sb("lastf", [P, BLOCKS])
        lasti = sb("lasti", [P, BLOCKS], I32)
        lastd = sb("lastd", [TP, TC], I32)
        key = sb("key", [TP, TC])
        tile_no = sb("tile_no", [TP, TC])
        ts_f = sb("ts_f", [P, SC])
        bs_f = sb("bs_f", [P, SC])
        s_no = sb("s_no", [P, SC])
        step_i = sb("step_i", [P, 3, SC], I32)
        rows_i = sb("rows_i", [1, 3, SPAD], I32)
        DRi = sb("DRi", [P, SC, P], I32)
        SRf = CATW[:, 0:SPAD].rearrange("p (c e) -> p c e", e=P)
        DLf = CATW[:, SPAD:2 * SPAD].rearrange("p (c e) -> p c e", e=P)
        SBf = H[:].rearrange("p b f -> p (b f)")[:, 0:SPAD].rearrange("p (c e) -> p c e", e=P)
        SPf = Y[:].rearrange("p b f -> p (b f)")[:, 0:SPAD].rearrange("p (c e) -> p c e", e=P)
        INf = CATW[:, 2 * SPAD:3 * SPAD].rearrange("p (c e) -> p c e", e=P)
        idx_s = sb("idx_s", [P, SPAD])
        dl_s = sb("dl_s", [P, SPAD])
        sp_s = sb("sp_s", [P, SPAD])
        sbk_s = sb("sbk_s", [P, SPAD])
        in_s = sb("in_s", [P, SPAD])
        idx = sb("idx", [P, SLOTS, G], I32)
        gat = sb("gat", [P, SLOTS, G, F])
        msg = sb("msg", [P, SLOTS, G, F])
        oh = sb("oh", [P, SLOTS, G, P])
        ohb = sb("ohb", [P, SLOTS, G, P], BF16)
        oha = sb("oha", [P, SLOTS, G, BLOCKS], BF16)
        row = sb("row", [P, SLOTS, G, P])
        srow = sb("srow", [P, SLOTS, G, P])
        trash = sb("trash", [P, 1])
        iota_s = row[0:TP].rearrange("p b g e -> p (b g e)")[:, 0:SPAD]
        below = srow[0:TP].rearrange("p b g e -> p (b g e)")[:, 0:SPAD]
        SRi = oh[:].rearrange("p b g e -> p (b g e)")[:, 0:SPAD].rearrange("p (c e) -> p c e", e=P).bitcast(I32)
        rep = sb("rep", [P, SLOTS, G])
        repi = sb("repi", [P, SLOTS, G])
        usum = sb("usum", [P, G, F])
        usq = sb("usq", [P, G, F])
        sqt = sb("sqt", [P, G, F])
        bn = sb("bn", [P, 6, F])
        xt = sb("xt", [P, 2, BANK])
        lw = sb("lw", [EF32, F])

        psum = ctx.enter_context(nc.psum_tensor("psum", [P, 8, BANK], F32))
        pflat = psum[:].rearrange("p k n -> p (k n)")
        sums = pflat[:, 0:NW]
        sums3 = sums.rearrange("p (b f) -> p b f", f=F)
        edge_ps = psum[:, 7, :]
        edge3 = edge_ps.rearrange("p (g f) -> p g f", f=F)
        deg_ps = psum[:, 7, 0:BLOCKS]
        cnt_ps = psum[:, 7, 64:64 + BLOCKS]
        CNT0 = 7 * BANK + 64

        s_const = sem("s_const")
        s_zrow = sem("s_zrow")
        s_w = sem("s_w")
        s_x = sem("s_x")
        s_last = sem("s_last")
        s_tabz = sem("s_tabz")
        s_below = sem("s_below")
        s_tcount = sem("s_tcount")
        s_step = sem("s_step")
        s_rowst = sem("s_rowst")
        s_rows = sem("s_rows")
        s_tiles = sem("s_tiles")
        s_fields = sem("s_fields")
        s_rec = sem("s_rec")
        s_ptr = sem("s_ptr")
        s_pev = sem("s_pev")
        s_dve = sem("s_dve")
        s_lay = sem("s_lay")
        h2_ready = sem("h2_ready")
        added_before = sem("added_before")
        s_sq = sem("s_sq")
        s_tab = [sem(f"s_tab{k}") for k in range(4)]
        idx_ready = [sem(f"idx_ready{k}") for k in range(4)]
        gathered = [[sem(f"gathered{k}_{b}") for b in range(SLOTS)] for k in range(4)]
        rows_in = [[sem(f"rows_in{k}_{b}") for b in range(SLOTS)] for k in range(4)]
        srows_in = [sem(f"srows_in_{b}") for b in range(SLOTS)]
        edge_done = [sem(f"edge_done{k}") for k in range(4)]
        summed = [sem(f"summed{k}") for k in range(4)]
        oh_ready = [sem(f"oh_ready{k}") for k in range(4)]
        deg_ready = sem("deg_ready")
        msg_ready = [sem(f"msg_ready{k}") for k in range(4)]
        scattered = [sem(f"scattered{k}") for k in range(4)]
        dup_ready = sem("dup_ready")
        dup_done = sem("dup_done")
        addi_ready = sem("addi_ready")
        add_ready = sem("add_ready")
        added = [sem(f"added{k}") for k in range(TABLES)]
        s_grp = sem("s_grp")
        s_src = sem("s_src")
        t_ps = sem("t_ps")
        t_sb = sem("t_sb")
        l_ps = sem("l_ps")
        l_out = sem("l_out")
        s_h = sem("s_h")
        s_min = sem("s_min")
        s_exp = sem("s_exp")
        s_lw = sem("s_lw")
        s_cnt1 = sem("s_cnt1")
        s_cnt2 = sem("s_cnt2")
        s_lasti = sem("s_lasti")
        s_eg = sem("s_eg")
        s_tin = [sem(f"s_tin{b}") for b in range(2)]
        s_tuse = sem("s_tuse")
        s_bn = sem("s_bn")
        s_bnp = sem("s_bnp")
        root_asked = sem("root_asked")
        root_taken = sem("root_taken")
        s_fin = sem("s_fin")
        s_out = sem("s_out")

        block = ctx.enter_context(nc.Block())

        L0A, L0B, L1A, L2A, L3A = 0, 1, 2, 2 + LAYERS, 3 + LAYERS

        @block.sync
        def _(sp):
            def bcast(dst_t, v):
                sp.dma_start(dst_t, v.rearrange("(a n) -> a n", a=1).broadcast_to([P, v.shape[0]])).then_inc(s_w, 16)

            sp.dma_start(lastd[:], last).then_inc(s_last, 16)
            sp.dma_start(X[:], x.rearrange("(b p) f -> p b f", p=P)).then_inc(s_x, 16)
            for t, v in ((w0[0:F, :], wl), (w0[F:P, :], wr), (w0e[0:EF16, :], we),
                         (w0e[EF16:EF16 + 1, :], be.rearrange("(a n) -> a n", a=1)),
                         (nnw_all[:].rearrange("p (l f) -> p l f", f=F), nnw.rearrange("l p f -> p l f")),
                         (linw_all[:, 0:LAYERS * F].rearrange("p (l f) -> p l f", f=F), linw.rearrange("l p f -> p l f")),
                         (w2_sb[:], w2), (w3a_sb[:], w3a), (w3b_sb[:], w3b)):
                sp.dma_start(t, v).then_inc(s_w, 16)
            for t, v in ((bl_b[:], bl), (b2_b[:], b2), (b3_b[:], b3), (gamma_b[:], gamma), (beta_b[:], beta),
                         (nnb_b[:], nnb.rearrange("l f -> (l f)")), (linb_b[:, 0:LAYERS * F], linb.rearrange("l f -> (l f)"))):
                bcast(t, v)
            sp.wait_ge(s_zrow, 1)
            for k in range(TABLES):
                r = (NPAD + TRASH) // P
                sp.dma_start(tables[k].rearrange("(p r) f -> p r f", r=r),
                             zrow[:].rearrange("p (a f) -> p a f", a=1).broadcast_to([P, r, F])).then_inc(s_tabz, 16)
            sp.wait_ge(s_step, 1)
            sp.dma_start(row_scratch.rearrange("k (c p) -> p k c", p=P), step_i[:],
                         allow_slow_non_contiguous=True).then_inc(s_rowst, 16)
            sp.wait_ge(s_rowst, 16)
            sp.dma_start(rows_i[0:1, :, :], row_scratch.rearrange("(a k) s -> a k s", a=1)).then_inc(s_rows, 16)
            sp.wait_ge(s_fields, 1)
            sp.dma_start(dl_rows.rearrange("(c p) e -> p c e", p=P), DLf).then_inc(s_rec, 16)
            sp.dma_start(sr_rows.rearrange("(c p) e -> p c e", p=P), SRf).then_inc(s_rec, 16)

            sp.wait_ge(s_rows, 16)
            tile_regs = [sp.alloc_register(f"tile{k}") for k in range(G)]

            def attributes(k, table, nf, n0):
                with sp.Fori(0, ITERS) as i:
                    for b in range(SLOTS):
                        g = i * SLOTS + b
                        sp.load(tile_regs, rows_i[0:1, 0, bass.ds(g * G, G)])
                        sp.wait_ge(edge_done[k], n0 + free(g))
                        for j in range(G):
                            t = sp.snap(tile_regs[j], min_val=0, max_val=LAST_T)
                            sp.dma_start(row[0:nf, b, j, :],
                                         table[bass.ds(t, 1)].rearrange("a f e -> (a f) e")).then_inc(rows_in[k][b], 16)

            def store_table(n):
                sp.wait_ge(s_h, n)
                sp.dma_start(node_table.rearrange("(b p) f -> p b f", p=P), SQ2).then_inc(s_tab[1], 16)

            store_table(1)
            with sp.Fori(0, LAYERS) as l:
                attributes(1, ea32t, EF32, l * GROUPS)
                store_table(l + 2)
            sp.wait_ge(s_rec, 32)
            with sp.Fori(0, ITERS) as i:
                for b in range(SLOTS):
                    g = i * SLOTS + b
                    sp.wait_ge(dup_done, free(g))
                    for t, v, s in ((row, dl_rows, rows_in[2][b]), (srow, sr_rows, srows_in[b])):
                        sp.dma_start(t[:, b].rearrange("p g e -> p (g e)"),
                                     v[bass.ds(g * G, G), :].rearrange("(a s) e -> a (s e)", a=1)
                                     .broadcast_to([P, G * P])).then_inc(s, 16)
            for k in range(TABLES):
                sp.wait_ge(added[k], 16 * GROUPS)
            for k in range(TABLES):
                if k >= 2:
                    sp.wait_ge(s_tuse, k - 1)
                sp.dma_start((Y[:], SQ)[k % 2],
                             tables[k][0:NPAD, :].rearrange("(b p) f -> p b f", p=P)).then_inc(s_tin[k % 2], 16)
            sp.wait_ge(s_h, LAYERS + 2)
            sp.dma_start(node_table.rearrange("(b p) f -> p b f", p=P), H[:]).then_inc(s_tab[3], 16)
            attributes(3, ea16t, EF16, 0)
            sp.wait_ge(s_fin, 1)
            full = NODES // P
            sp.dma_start(out[0:full * P, :].rearrange("(b p) f -> p b f", p=P), X[:, 0:full, :]).then_inc(s_out, 16)
            sp.dma_start(out[full * P:NODES, :], X[0:NODES - full * P, full, :]).then_inc(s_out, 16)
            sp.wait_ge(s_out, 32)

        @block.gpsimd
        def _(pool):
            pool.iota(iota_row[:], pattern=[[1, P]], base=0, channel_multiplier=0,
                      allow_small_or_imprecise_dtypes=True).then_inc(s_const, 1)
            pool.iota(iota_p[:], pattern=[[1, 1]], base=0, channel_multiplier=1,
                      allow_small_or_imprecise_dtypes=True).then_inc(s_const, 1)
            pool.iota(iota_s, pattern=[[1, SPAD]], base=0, channel_multiplier=0,
                      allow_small_or_imprecise_dtypes=True).then_inc(s_const, 1)
            pool.iota(tile_no[:], pattern=[[1, TC]], base=0, channel_multiplier=TC,
                      allow_small_or_imprecise_dtypes=True).then_inc(s_const, 1)
            pool.iota(s_no[:], pattern=[[P, SC]], base=0, channel_multiplier=1,
                      allow_small_or_imprecise_dtypes=True).then_inc(s_const, 1)
            pool.wait_ge(s_step, 1)
            for c in range(SC):
                for t, v in ((SRi, src), (DRi, dst)):
                    pool.indirect_dma_start(t[:, c, :], None, v,
                                            bass.IndirectOffsetOnAxis(step_i[:, 0, c:c + 1], 0)).then_inc(s_tiles, 16)

            def gathers(k, table, n0, d0, consumed):
                with pool.Fori(0, ITERS) as i:
                    for b in range(SLOTS):
                        g = i * SLOTS + b
                        pool.wait_ge(consumed, n0 + free(g))
                        pool.wait_ge(idx_ready[k], d0 * (GROUPS + SLOTS) + (g + 1))
                        pool.nop(nofuse=True)
                        for j in range(G):
                            pool.indirect_dma_start(gat[:, b, j, :], None, table,
                                                    bass.IndirectOffsetOnAxis(idx[:, b, j:j + 1], 0)
                                                    ).then_inc(gathered[k][b], 16)

            gathers(0, x, 0, 0, scattered[0])
            pool.wait_ge(s_lasti, 1)
            for c in range(BLOCKS):
                pool.indirect_dma_start(EG[:, c, :], None, ea16,
                                        bass.IndirectOffsetOnAxis(lasti[:, c:c + 1], 0)).then_inc(s_eg, 16)
            with pool.Fori(0, LAYERS) as l:
                pool.wait_ge(s_tab[1], l * 16 + 16)
                pool.nop(nofuse=True)
                gathers(1, node_table, l * GROUPS, l, summed[1])
            pool.wait_ge(s_tabz, 16 * TABLES)

            def additions(i, b):
                g = i * SLOTS + b
                pool.wait_ge(addi_ready, g + 1)
                pool.wait_ge(add_ready, done(g))
                for j in range(G):
                    if not isinstance(g, int) or g:
                        pool.wait_ge(added[j], g * 16)
                        pool.nop(nofuse=True)
                    if j == G - 1:
                        pool.sem_inc(added_before, 1)
                    pool.indirect_dma_start(tables[j], bass.IndirectOffsetOnAxis(idx[:, b, j:j + 1], 0),
                                            gat[:, b, j, :], None, compute_op=ALU.add).then_inc(added[j], 16)

            pool.sem_inc(added_before, 1)
            for b in range(SLOTS):
                additions(0, b)
            with pool.Fori(1, ITERS) as i:
                for b in range(SLOTS):
                    additions(i, b)
            pool.wait_ge(s_tab[3], 16)
            gathers(3, node_table, 0, 0, summed[3])

        @block.scalar
        def _(act):
            for s in (t_sb, msg_ready[2], add_ready):
                act.sem_inc(s, SLOTS)
            fields = ((SRf, idx_s), (DLf, dl_s), (SPf, sp_s), (SBf, sbk_s), (INf, in_s))
            act.wait_ge(s_fields, 1)
            n = 0
            for f, to in fields:
                for c0 in range(0, SC, 4):
                    n += 1
                    w = min(4, SC - c0) * P
                    act.wait_ge(s_ptr, n)
                    act.activation(to[:, c0 * P:c0 * P + w], psum[:, (n - 1) % 4, 0:w], ACT.Copy).then_inc(s_pev, 1)

            def indices(k, g, b):
                act.activation(idx[:, b, :], idx_s[:, bass.ds(g * G, G)], ACT.Copy).then_inc(idx_ready[k], 1)

            roots = [0]

            def root(v):
                roots[0] += 1
                act.wait_ge(root_asked, roots[0])
                act.activation(v, v, ACT.Sqrt).then_inc(root_taken, 1)

            def transposed_rows(call, rows):
                for j in range(NCH):
                    n = call * NCH + j
                    w = CHUNKS[j] * P
                    act.wait_ge(t_ps, n + 1 + SLOTS)
                    act.wait_ge(l_ps, n + 1)
                    act.activation(xt[0:rows, j % 2, 0:w], psum[0:rows, j % 2, 0:w], ACT.Copy).then_inc(t_sb, 1)

            act.wait_ge(s_pev, 20)
            for b in range(SLOTS):
                indices(0, b, b)
            with act.Fori(0, ITERS) as i:
                for b in range(SLOTS):
                    act.wait_ge(gathered[0][b], (i + 1) * (16 * G))
                    indices(0, i * SLOTS + (b + SLOTS), b)
            transposed_rows(L0A, P)
            transposed_rows(L0B, EF16 + 1)
            root(stat[:, 1, :])

            def relu_pass(k, l, n0):
                for b in range(SLOTS):
                    indices(k, b, b)
                with act.Fori(0, ITERS) as i:
                    for b in range(SLOTS):
                        g = i * SLOTS + b
                        act.wait_ge(summed[k], n0 + done(g))
                        m = msg[:, b].rearrange("p g f -> p (g f)")
                        act.activation(m, m, ACT.Relu).then_inc(msg_ready[k], 1)
                        act.wait_ge(gathered[k][b], (l * ITERS + i + 1) * (16 * G))
                        indices(k, g + SLOTS, b)

            with act.Fori(0, LAYERS) as l:
                relu_pass(1, l, l * GROUPS)
                transposed_rows(L1A + l, F)
                act.wait_ge(s_min, l + 1)
                act.activation(SQ, SQ, ACT.Exp).then_inc(s_exp, 1)
            root(stat[:, 1, :])
            root(dinv[:])
            transposed_rows(L2A, F)
            with act.Fori(0, ITERS) as i:
                for b in range(SLOTS):
                    g = i * SLOTS + b
                    act.wait_ge(edge_done[2], done(g))
                    act.wait_ge(dup_done, free(g))
                    act.activation(msg[:, b].rearrange("p g f -> p (g f)"), psum[:, b, :], ACT.Copy
                                   ).then_inc(msg_ready[2], 1)
                    act.wait_ge(dup_done, done(g))
                    act.wait_ge(added_before, free(g))
                    act.activation(gat[:, b].rearrange("p g f -> p (g f)"), psum[:, 2 + b, :], ACT.Copy
                                   ).then_inc(add_ready, 1)
            root(stat[:, 1, :])
            transposed_rows(L3A, F)
            relu_pass(3, 0, 0)
            root(bn[:, 4, :])
            root(stat[:, 1, :])

        @block.vector
        def _(dve):
            for k in (1, 3):
                dve.sem_inc(summed[k], SLOTS)
            dve.sem_inc(l_out, SLOTS)
            chain = [0]

            def link(ins):
                chain[0] += 1
                ins.then_inc(s_dve, 1)
                dve.wait_ge(s_dve, chain[0])

            def b3d(t, n=F):
                return t.rearrange("p (b o) -> p b o", o=1).broadcast_to([P, BLOCKS, n])

            def f3d(t, n=BLOCKS):
                return t.rearrange("p (o f) -> p o f", o=1).broadcast_to([P, n, F])

            dve.memset(zrow[:], 0.0)
            dve.memset(linw_all[:, LAYERS * F:], 0.0)
            dve.memset(linb_b[:, LAYERS * F:], 0.0)
            dve.memset(zeros[:], 0.0)
            link(dve.memset(ones[:], 1.0))
            dve.wait_ge(s_const, 5)
            dve.sem_inc(s_zrow, 1)
            dve.tensor_scalar(upper[:], iota_row[:], iota_p[:], None, ALU.is_ge)
            dve.tensor_scalar(trash[:], iota_p[:], float(NPAD), None, ALU.add)
            dve.tensor_scalar(strict[:], iota_row[:], iota_p[:], None, ALU.is_gt)
            link(dve.tensor_scalar(ident[:], iota_row[:], iota_p[:], None, ALU.is_equal))
            dve.wait_ge(s_last, 16)
            link(dve.tensor_scalar(lastd[:], lastd[:], 7, None, ALU.arith_shift_right))
            link(dve.tensor_copy(key[:], lastd[:]))
            link(dve.tensor_tensor(key[:], key[:], tile_no[:], ALU.add))
            link(dve.tensor_scalar(below, iota_s, key[:, 0:1], None, ALU.is_gt))
            for c in range(1, TC):
                ins = dve.scalar_tensor_tensor(out=below, in0=iota_s, scalar=key[:, c:c + 1], in1=below,
                                               op0=ALU.is_gt, op1=ALU.add)
                link(ins) if c < TC - 1 else ins.then_inc(s_below, 1)
            dve.wait_ge(s_tcount, 1)
            link(dve.tensor_copy(ts_f[:], psum[:, 0, 0:SC]))
            link(dve.tensor_tensor(bs_f[:], s_no[:], ts_f[:], ALU.subtract))
            link(dve.tensor_scalar(bs_f[:], bs_f[:], float(BLOCKS - 1), None, ALU.min))
            link(dve.tensor_scalar(ts_f[:], ts_f[:], float(LAST_T), None, ALU.min))
            link(dve.tensor_copy(step_i[:, 0, :], ts_f[:]))
            link(dve.tensor_copy(step_i[:, 1, :], bs_f[:]))
            dve.tensor_scalar(step_i[:, 2, :], bs_f[:], float(F), None, ALU.mult).then_inc(s_step, 1)
            dve.wait_ge(s_tiles, 16 * 2 * SC)
            link(dve.tensor_copy(SRf, SRi))
            link(dve.tensor_copy(DLf, DRi[:]))
            link(dve.tensor_scalar(INf, DLf, float(NODES), -1e6, ALU.is_ge, ALU.mult))
            link(dve.tensor_tensor(DLf, DLf, INf, ALU.add))
            link(dve.tensor_scalar(bs_f[:], bs_f[:], float(P), None, ALU.mult))
            link(dve.tensor_tensor(DLf, DLf, bs_f[:].rearrange("p (c o) -> p c o", o=1).broadcast_to([P, SC, P]),
                                   ALU.subtract))
            link(dve.tensor_scalar(DRi[:], SRi, 7, None, ALU.arith_shift_right))
            link(dve.tensor_copy(SBf, DRi[:]))
            link(dve.tensor_scalar(DRi[:], SRi, P - 1, None, ALU.bitwise_and))
            link(dve.tensor_copy(SPf, DRi[:]))
            link(dve.tensor_scalar(INf, DLf, 0.0, None, ALU.is_ge))
            link(dve.scalar_tensor_tensor(out=INf, in0=DLf, scalar=float(P), in1=INf, op0=ALU.is_lt, op1=ALU.mult))
            link(dve.scalar_tensor_tensor(out=SPf, in0=SPf, scalar=1.0, in1=INf, op0=ALU.add, op1=ALU.mult))
            dve.tensor_scalar(SPf, SPf, -1.0, None, ALU.add).then_inc(s_fields, 1)
            dve.wait_ge(s_pev, 20)

            def onehot(k, n0, g, b):
                dve.wait_ge(scattered[k], n0 + free(g))
                ins = dve.tensor_tensor(oh[:, b],
                                        iota_row[:].rearrange("p (o n) -> p o n", o=1).broadcast_to([P, G, P]),
                                        dl_s[:, bass.ds(g * G, G)].rearrange("p (g o) -> p g o", o=1)
                                        .broadcast_to([P, G, P]), ALU.is_equal)
                ins.then_inc(oh_ready[k], 1)

            with dve.Fori(0, ITERS) as i:
                for b in range(SLOTS):
                    g = i * SLOTS + b
                    onehot(0, 0, g, b)
                    dve.tensor_tensor(ohb[:, b],
                                      iota_row[:].rearrange("p (o n) -> p o n", o=1).broadcast_to([P, G, P]),
                                      sp_s[:, bass.ds(g * G, G)].rearrange("p (g o) -> p g o", o=1)
                                      .broadcast_to([P, G, P]), ALU.is_equal)
                    dve.tensor_tensor(oha[:, b],
                                      iota_row[:, 0:BLOCKS].rearrange("p (o n) -> p o n", o=1)
                                      .broadcast_to([P, G, BLOCKS]),
                                      sbk_s[:, bass.ds(g * G, G)].rearrange("p (g o) -> p g o", o=1)
                                      .broadcast_to([P, G, BLOCKS]), ALU.is_equal).then_inc(deg_ready, 1)

            def take(call, j, addend, o):
                n = call * NCH + j
                b0, b1 = START[j], START[j] + CHUNKS[j]
                dve.wait_ge(l_ps, n + 1 + SLOTS)
                v = psum[:, 2 + j % 2, 0:(b1 - b0) * F].rearrange("p (b f) -> p b f", f=F)
                if addend is None:
                    ins = dve.tensor_copy(o[:, b0:b1, :], v)
                else:
                    a = addend[:, b0:b1, :] if addend.shape[1] == BLOCKS else addend[:, 0:b1 - b0, :]
                    ins = dve.tensor_tensor(o[:, b0:b1, :], v, a, ALU.add)
                ins.then_inc(l_out, 1)
                if j == NCH - 1:
                    dve.wait_ge(l_out, n + 1 + SLOTS)

            roots = [0]

            def rsqrt(v, add):
                roots[0] += 1
                dve.tensor_scalar(v, v, add, None, ALU.add).then_inc(root_asked, 1)
                dve.wait_ge(root_taken, roots[0])
                link(dve.reciprocal(v, v))

            def layernorm(v, link):
                link(dve.tensor_reduce(stat[:, 0, :], v, AX.X, ALU.add))
                link(dve.tensor_scalar(stat[:, 0, :], stat[:, 0, :], -1.0 / F, None, ALU.mult))
                link(dve.tensor_tensor(v, v, b3d(stat[:, 0, :]), ALU.add))
                link(dve.tensor_tensor(SQ, v, v, ALU.mult))
                link(dve.tensor_reduce(stat[:, 1, :], SQ, AX.X, ALU.add))
                link(dve.tensor_scalar(stat[:, 1, :], stat[:, 1, :], 1.0 / F, None, ALU.mult))
                rsqrt(stat[:, 1, :], EPS)
                link(dve.tensor_tensor(v, v, b3d(stat[:, 1, :]), ALU.mult))

            dve.wait_ge(scattered[0], GROUPS + SLOTS)
            link(dve.tensor_copy(cnt[:], cnt_ps))
            dve.tensor_copy(deg[:], deg_ps).then_inc(s_cnt1, 1)
            link(dve.tensor_scalar(rcnt[:], cnt[:], 1.0, None, ALU.max))
            link(dve.reciprocal(rcnt[:], rcnt[:]))
            dve.wait_ge(s_cnt2, 1)
            dve.tensor_copy(cntT[:], psum[0:BLOCKS, 7, 128:256]).then_inc(s_cnt1, 1)
            dve.wait_ge(s_cnt2, 2)
            dve.tensor_copy(cntX[:], psum[:, 7, 256:256 + BLOCKS]).then_inc(s_cnt1, 1)
            dve.wait_ge(s_cnt2, 3)
            link(dve.tensor_scalar(lastf[:], psum[:, 7, 384:384 + BLOCKS], -1.0, 0.0, ALU.add, ALU.max))
            dve.tensor_copy(lasti[:], lastf[:]).then_inc(s_lasti, 1)
            dve.wait_ge(s_rec, 32)
            link(dve.tensor_tensor(CAT[:, :, 0:F], sums3, b3d(rcnt[:]), ALU.mult))
            dve.wait_ge(s_x, 16)
            dve.wait_ge(s_w, 16 * 16)
            dve.tensor_copy(CAT[:, :, F:2 * F], X[:]).then_inc(s_src, 1)
            for j in range(NCH):
                take(L0A, j, f3d(bl_b[:], CH), Y[:])
            link(dve.tensor_scalar(E17[:, :, EF16:EF16 + 1].rearrange("p b o -> p (b o)"), cnt[:], 0.0, None,
                                   ALU.is_gt))
            dve.wait_ge(s_eg, 16 * BLOCKS)
            dve.tensor_tensor(E17[:, :, 0:EF16], EG[:], E17[:, :, EF16:EF16 + 1].broadcast_to([P, BLOCKS, EF16]),
                              ALU.mult).then_inc(s_src, 1)
            for j in range(NCH):
                take(L0B, j, Y[:], Y[:])
            link(dve.tensor_tensor(X[:], X[:], Y[:], ALU.add))
            layernorm(X[:], link)
            link(dve.tensor_copy(H[:], X[:]))
            link(dve.tensor_copy(lw[:], linw_all[:, 0:F]))
            dve.tensor_tensor(SQ2, H[:], f3d(linb_b[:, 0:F]), ALU.add).then_inc(s_h, 1)

            with dve.Fori(0, LAYERS) as l:
                n0 = l * GROUPS
                with dve.Fori(0, ITERS) as i:
                    for b in range(SLOTS):
                        g = i * SLOTS + b
                        onehot(1, n0, g, b)
                        dve.wait_ge(edge_done[1], n0 + done(g))
                        dve.wait_ge(gathered[1][b], (l * ITERS + i + 1) * (16 * G))
                        dve.tensor_tensor(msg[:, b], edge3, gat[:, b], ALU.add).then_inc(summed[1], 1)
                LINKS = 2
                m = [0]

                def lay(ins):
                    m[0] += 1
                    ins.then_inc(s_lay, 1)
                    dve.wait_ge(s_lay, l * LINKS + m[0])

                dve.wait_ge(scattered[1], n0 + (GROUPS + SLOTS))
                dve.tensor_tensor(H[:], H[:], sums3, ALU.add).then_inc(s_src, 1)
                for j in range(NCH):
                    take(L1A + l, j, nnb_b[:, bass.ds(l * F, F)].rearrange("p (o f) -> p o f", o=1)
                         .broadcast_to([P, CH, F]), Y[:])
                dve.tensor_scalar(SQ, Y[:], 0.0, None, ALU.min).then_inc(s_min, 1)
                dve.wait_ge(s_exp, l + 1)
                lay(dve.scalar_tensor_tensor(out=H[:], in0=SQ, scalar=-1.0, in1=Y[:], op0=ALU.add, op1=ALU.max))
                nl = l + 1
                lay(dve.tensor_copy(lw[:], linw_all[:, bass.ds(nl * F, F)]))
                dve.wait_ge(s_tab[1], l * 16 + 16)
                dve.tensor_tensor(SQ2, H[:], linb_b[:, bass.ds(nl * F, F)].rearrange("p (o f) -> p o f", o=1)
                                  .broadcast_to([P, BLOCKS, F]), ALU.add).then_inc(s_h, 1)

            link(dve.tensor_tensor(X[:], X[:], H[:], ALU.add))
            layernorm(X[:], link)
            link(dve.tensor_copy(dinv[:], deg[:]))
            rsqrt(dinv[:], 1.0)
            dve.sem_inc(s_src, 1)
            for j in range(NCH):
                take(L2A, j, None, H[:])
            dve.wait_ge(s_src, 2 + LAYERS + 1)
            dve.tensor_tensor(H[:], H[:], b3d(dinv[:]), ALU.mult).then_inc(h2_ready, 1)
            with dve.Fori(0, ITERS) as i:
                for b in range(SLOTS):
                    g = i * SLOTS + b
                    dve.wait_ge(rows_in[2][b], (i + 1) * 16)
                    dve.wait_ge(edge_done[2], free(g))
                    dve.tensor_scalar(oh[:, b], row[:, b], iota_p[:], None, ALU.is_equal).then_inc(oh_ready[2], 1)
                    dve.wait_ge(srows_in[b], (i + 1) * 16)
                    for j in range(G):
                        ins = dve.scalar_tensor_tensor(out=srow[:, b, j, :], in0=srow[:, b, j, :],
                                                       scalar=idx_s[:, bass.ds(g * G + j, 1)], in1=upper[:],
                                                       op0=ALU.is_equal, op1=ALU.mult, accum_out=rep[:, b, j:j + 1])
                    ins.then_inc(dup_ready, 1)
                    dve.tensor_scalar(repi[:, b, :], idx_s[:, bass.ds(g * G, G)], trash[:], None,
                                      ALU.subtract).then_inc(s_grp, 1)
                    dve.wait_ge(dup_ready, g + 1)
                    dve.tensor_scalar(rep[:, b, :], rep[:, b, :], 1.5, None, ALU.is_gt).then_inc(s_grp, 1)
                    dve.wait_ge(s_grp, g * 3 + 2)
                    dve.tensor_tensor(repi[:, b, :], repi[:, b, :], rep[:, b, :], ALU.mult).then_inc(s_grp, 1)
                    dve.wait_ge(s_grp, g * 3 + 3)
                    dve.wait_ge(added_before, free(g))
                    dve.tensor_tensor(idx[:, b, :], idx_s[:, bass.ds(g * G, G)], repi[:, b, :],
                                      ALU.subtract).then_inc(addi_ready, 1)
            for k in range(TABLES):
                dve.wait_ge(s_tin[k % 2], 16 * (k // 2 + 1))
                if k:
                    dve.wait_ge(s_tuse, k)
                dve.tensor_tensor(H[:], H[:], (Y[:], SQ)[k % 2], ALU.add).then_inc(s_tuse, 1)
            dve.wait_ge(s_tuse, TABLES)
            link(dve.tensor_tensor(H[:], H[:], b3d(dinv[:]), ALU.mult))
            link(dve.tensor_tensor(H[:], H[:], f3d(b2_b[:]), ALU.add))
            link(dve.tensor_tensor(X[:], X[:], H[:], ALU.add))
            layernorm(X[:], link)

            link(dve.memset(usq[:], 0.0))
            dve.memset(usum[:], 0.0).then_inc(s_src, 1)
            dve.wait_ge(s_src, 4 + LAYERS)
            for j in range(NCH):
                take(L3A, j, f3d(b3_b[:], CH), H[:])
            dve.sem_inc(s_h, 1)
            with dve.Fori(0, ITERS) as i:
                for b in range(SLOTS):
                    g = i * SLOTS + b
                    onehot(3, 0, g, b)
                    dve.wait_ge(edge_done[3], done(g))
                    dve.wait_ge(gathered[3][b], (i + 1) * (16 * G))
                    dve.tensor_tensor(msg[:, b], edge3, gat[:, b], ALU.add).then_inc(summed[3], 1)
                    dve.wait_ge(msg_ready[3], g + 1)
                    dve.tensor_tensor(sqt[:], msg[:, b], in_s[:, bass.ds(g * G, G)]
                                      .rearrange("p (g o) -> p g o", o=1).broadcast_to([P, G, F]),
                                      ALU.mult).then_inc(s_sq, 1)
                    dve.wait_ge(s_sq, g * 4 + 1)
                    dve.tensor_tensor(usum[:], usum[:], sqt[:], ALU.add).then_inc(s_sq, 1)
                    dve.wait_ge(s_sq, g * 4 + 2)
                    dve.tensor_tensor(sqt[:], sqt[:], msg[:, b], ALU.mult).then_inc(s_sq, 1)
                    dve.wait_ge(s_sq, g * 4 + 3)
                    dve.tensor_tensor(usq[:], usq[:], sqt[:], ALU.add).then_inc(s_sq, 1)
                    dve.wait_ge(s_sq, g * 4 + 4)
            dve.wait_ge(scattered[3], GROUPS + SLOTS)
            dve.tensor_copy(Y[:], sums3).then_inc(s_bn, 1)
            dve.wait_ge(s_bn, 1)
            dve.wait_ge(s_bnp, 1)
            MEAN, M2, A, C, T1 = (bn[:, k, :] for k in range(5))
            link(dve.tensor_reduce(MEAN, psum[:, 7, :].rearrange("p (g f) -> p f g", f=F), AX.X, ALU.add))
            link(dve.tensor_reduce(M2, psum[:, 0, :].rearrange("p (g f) -> p f g", f=F), AX.X, ALU.add))
            link(dve.tensor_scalar(MEAN, MEAN, 1.0 / EDGES, None, ALU.mult))
            link(dve.tensor_tensor(T1, MEAN, MEAN, ALU.mult))
            link(dve.scalar_tensor_tensor(out=T1, in0=M2, scalar=1.0 / EDGES, in1=T1, op0=ALU.mult, op1=ALU.subtract))
            link(dve.tensor_scalar(T1, T1, 0.0, None, ALU.max))
            rsqrt(T1, EPS)
            link(dve.tensor_tensor(A, gamma_b[:], T1, ALU.mult))
            link(dve.tensor_tensor(C, MEAN, A, ALU.mult))
            link(dve.tensor_tensor(C, beta_b[:], C, ALU.subtract))
            link(dve.tensor_tensor(Y[:], Y[:], f3d(A), ALU.mult))
            link(dve.tensor_tensor(SQ, b3d(cnt[:]), f3d(C), ALU.mult))
            link(dve.tensor_tensor(Y[:], Y[:], SQ, ALU.add))
            link(dve.tensor_tensor(Y[:], Y[:], b3d(rcnt[:]), ALU.mult))
            link(dve.scalar_tensor_tensor(out=X[:], in0=X[:], scalar=2.0, in1=Y[:], op0=ALU.mult, op1=ALU.add))
            layernorm(X[:], link)
            dve.sem_inc(s_fin, 1)

        @block.tensor
        def _(pe):
            for s in (scattered[0], scattered[1], scattered[3], edge_done[1], edge_done[2], edge_done[3],
                      dup_done, t_ps, l_ps):
                pe.sem_inc(s, SLOTS)
            pe.wait_ge(s_below, 1)
            for c in range(SC):
                ins = pe.matmul(psum[:, 0, c:c + 1], below[:, c * P:(c + 1) * P], ones[0:TP, 0:1], start=True, stop=True)
            ins.then_inc(s_tcount, 1)
            pe.wait_ge(s_fields, 1)
            n = 0
            for f in (SRf, DLf, SPf, SBf, INf):
                for c0 in range(0, SC, 4):
                    n += 1
                    if n > 4:
                        pe.wait_ge(s_pev, n - 4)
                    for c in range(c0, min(c0 + 4, SC)):
                        ins = pe.transpose(psum[:, (n - 1) % 4, (c - c0) * P:(c - c0 + 1) * P], f[:, c, :], ident[:])
                    ins.then_inc(s_ptr, 1)
            pe.wait_ge(s_w, 16 * 16)
            pe.wait_ge(s_rows, 16)
            pe.wait_ge(s_pev, 20)
            col_regs = [pe.alloc_register(f"col{k}") for k in range(G)]
            blk_regs = [pe.alloc_register(f"blk{k}") for k in range(G)]

            def zero_sums(banks):
                for k in banks:
                    pe.matmul(psum[:, k, :], zeros[:, 0:P], zeros[:], start=True, stop=False, skip_group_check=True)

            def columns(g):
                pe.load(col_regs, rows_i[0:1, 2, bass.ds(g * G, G)])
                return [pe.snap(r, min_val=0, max_val=NW - F) for r in col_regs]

            def node_product(call, src, K, W, ready):
                pe.wait_ge(s_src, ready)

                def turn(j):
                    n = call * NCH + j
                    pe.wait_ge(t_sb, free(n))
                    pe.nop(nofuse=True)
                    for q in range(CHUNKS[j]):
                        ins = pe.transpose(psum[0:K, j % 2, q * P:(q + 1) * P], src[:, START[j] + q, :], ident[:])
                    ins.then_inc(t_ps, 1)

                def multiply(j):
                    n = call * NCH + j
                    pe.wait_ge(t_sb, done(n))
                    pe.wait_ge(l_out, free(n))
                    pe.nop(nofuse=True)
                    for q in range(CHUNKS[j]):
                        ins = pe.matmul(psum[:, 2 + j % 2, q * F:(q + 1) * F], xt[0:K, j % 2, q * P:(q + 1) * P], W,
                                        start=True, stop=True)
                    ins.then_inc(l_ps, 1)

                turn(0)
                for j in range(NCH):
                    if j + 1 < NCH:
                        turn(j + 1)
                    multiply(j)
                pe.wait_ge(l_out, done(call * NCH + (NCH - 1)))

            zero_sums(range(8))
            with pe.Fori(0, ITERS) as i:
                for b in range(SLOTS):
                    g = i * SLOTS + b
                    cols = columns(g)
                    pe.load(blk_regs, rows_i[0:1, 1, bass.ds(g * G, G)])
                    pe.wait_ge(oh_ready[0], g + 1)
                    pe.wait_ge(deg_ready, g + 1)
                    for j in range(G):
                        pe.matmul(deg_ps, ohb[:, b, j, :], oha[:, b, j, :], start=False, stop=False,
                                  skip_group_check=True)
                        blk = pe.snap(blk_regs[j], min_val=0, max_val=BLOCKS - 1)
                        pe.matmul(pflat[:, bass.ds(blk + CNT0, 1)], oh[:, b, j, :], ones[:, 0:1], start=False,
                                  stop=False, skip_group_check=True)
                    pe.wait_ge(gathered[0][b], (i + 1) * (16 * G))
                    for j in range(G):
                        ins = pe.matmul(pflat[:, bass.ds(cols[j], F)], oh[:, b, j, :], gat[:, b, j, :], start=False,
                                        stop=False, skip_group_check=True)
                    ins.then_inc(scattered[0], 1)
            pe.wait_ge(s_cnt1, 1)
            pe.transpose(psum[0:BLOCKS, 7, 128:256], cnt[:], ident[:]).then_inc(s_cnt2, 1)
            pe.wait_ge(s_cnt1, 2)
            pe.matmul(psum[:, 7, 256:256 + BLOCKS], cntT[:], strict[0:BLOCKS, 0:BLOCKS], start=True,
                      stop=True).then_inc(s_cnt2, 1)
            pe.wait_ge(s_cnt1, 3)
            pe.matmul(psum[:, 7, 384:384 + BLOCKS], upper[:], cnt[:], start=True, stop=False)
            pe.matmul(psum[:, 7, 384:384 + BLOCKS], ones[:], cntX[:], start=False, stop=True).then_inc(s_cnt2, 1)
            node_product(L0A, CAT, P, w0[:], 1)
            node_product(L0B, E17, EF16 + 1, w0e[:], 2)

            def edge_pass(k, nf, W, l, n0):
                zero_sums(range(7))
                with pe.Fori(0, ITERS) as i:
                    for b in range(SLOTS):
                        g = i * SLOTS + b
                        cols = columns(g)
                        pe.wait_ge(rows_in[k][b], (l * ITERS + i + 1) * (16 * G))
                        pe.wait_ge(summed[k], n0 + (g + SLOTS))
                        for j in range(G):
                            ins = pe.matmul(edge3[:, j, :], row[0:nf, b, j, :], W, start=True, stop=True)
                        ins.then_inc(edge_done[k], 1)
                        pe.wait_ge(oh_ready[k], n0 + (g + 1))
                        pe.wait_ge(msg_ready[k], n0 + (g + 1))
                        for j in range(G):
                            ins = pe.matmul(pflat[:, bass.ds(cols[j], F)], oh[:, b, j, :], msg[:, b, j, :],
                                            start=False, stop=False, skip_group_check=True)
                        ins.then_inc(scattered[k], 1)

            with pe.Fori(0, LAYERS) as l:
                pe.wait_ge(s_h, l + 1)
                edge_pass(1, EF32, lw[:], l, l * GROUPS)
                node_product(L1A + l, H, F, nnw_all[:, bass.ds(l * F, F)], l + 3)
            node_product(L2A, X, F, w2_sb[:], 3 + LAYERS)
            pe.wait_ge(h2_ready, 1)
            with pe.Fori(0, ITERS) as i:
                for b in range(SLOTS):
                    g = i * SLOTS + b
                    cols = columns(g)
                    pe.wait_ge(oh_ready[2], g + 1)
                    pe.wait_ge(msg_ready[2], free(g))
                    for j in range(G):
                        ins = pe.matmul(psum[:, b, j * F:(j + 1) * F], oh[:, b, j, :],
                                        H[:].rearrange("p b f -> p (b f)")[:, bass.ds(cols[j], F)],
                                        start=True, stop=True)
                    ins.then_inc(edge_done[2], 1)
                    pe.wait_ge(dup_ready, g + 1)
                    pe.wait_ge(msg_ready[2], done(g))
                    pe.wait_ge(add_ready, free(g))
                    for j in range(G):
                        ins = pe.matmul(psum[:, 2 + b, j * F:(j + 1) * F], srow[:, b, j, :], msg[:, b, j, :],
                                        start=True, stop=True)
                    ins.then_inc(dup_done, 1)
            node_product(L3A, X, F, w3a_sb[:], 4 + LAYERS)
            edge_pass(3, EF16, w3b_sb[:], 0, 0)
            pe.wait_ge(s_bn, 1)
            pe.matmul(psum[:, 7, :], ones[:], usum[:].rearrange("p g f -> p (g f)"), start=True, stop=True)
            pe.matmul(psum[:, 0, :], ones[:], usq[:].rearrange("p g f -> p (g f)"), start=True,
                      stop=True).then_inc(s_bnp, 1)


def kernel(**inputs):
    import numpy as np
    import concourse.bacc as bacc
    from concourse import mybir as mb
    from concourse.bass_utils import run_bass_kernel_spmd

    def a(name):
        return np.ascontiguousarray(inputs[name])

    pad = TILES * P - EDGES

    def tiles(v, fill=0):
        return np.concatenate([v, np.full((pad,) + v.shape[1:], fill, v.dtype)]).reshape((TILES, P) + v.shape[1:])

    w3 = a("L3_gnn_W")
    arrays = {
        "x": np.concatenate([a("x"), np.zeros((NPAD - NODES, F), np.float32)]),
        "src": tiles(a("src"), NPAD - 1), "dst": tiles(a("dst"), NPAD - 1),
        "last": np.ascontiguousarray(tiles(a("dst"), NPAD - 1)[:, P - 1].reshape(TP, TC)),
        "ea16": a("edge_attr_16"),
        "ea16t": np.ascontiguousarray(tiles(a("edge_attr_16")).transpose(0, 2, 1)),
        "ea32t": np.ascontiguousarray(tiles(a("edge_attr_32")).transpose(0, 2, 1)),
        "wl": a("L0_gnn_W_l"), "bl": a("L0_gnn_b_l"), "wr": a("L0_gnn_W_r"), "we": a("L0_gnn_W_e"),
        "be": a("L0_gnn_b_e"), "nnw": a("L1_gnn_nn_w"), "nnb": a("L1_gnn_nn_b"), "linw": a("L1_gnn_lin_w"),
        "linb": a("L1_gnn_lin_b"), "w2": a("L2_gnn_weight"), "b2": a("L2_gnn_bias"),
        "w3a": np.ascontiguousarray(w3[:, 0:F].T), "w3b": np.ascontiguousarray(w3[:, F:].T), "b3": a("L3_gnn_b"),
        "gamma": a("L3_gnn_gamma"), "beta": a("L3_gnn_beta"),
    }
    nc = bacc.Bacc("TRN2", target_bir_lowering=False, num_devices=1)
    args = {n: nc.dram_tensor(n, v.shape, mb.dt.from_np(v.dtype), kind="ExternalInput").ap() for n, v in arrays.items()}
    out = nc.dram_tensor("out", (NODES, F), F32, kind="ExternalOutput").ap()
    gnn(nc, out=out, **args)
    r = run_bass_kernel_spmd(nc, [arrays], core_ids=[0])
    return r.results[0]["out"]
```
